# Optimizing a Trainium2 kernel written in Bass

```python
import numpy as np
import jax
import jax.numpy as jnp

def _softmax(x, axis=-1):
    return jax.nn.softmax(x, axis=axis)

def _gelu(x):
    return jax.nn.gelu(x, approximate=True)

def _silu(x):
    return jax.nn.silu(x)

def _sigmoid(x):
    return jax.nn.sigmoid(x)

def _layernorm(x, axis=-1, eps=1e-05):
    m = jnp.mean(x, axis=axis, keepdims=True)
    v = jnp.var(x, axis=axis, keepdims=True)
    return (x - m) / jnp.sqrt(v + eps)

def _scatter_add(tgt, idx, src, axis=0):
    return tgt.at[idx].add(src)

def _segment_sum(src, seg, n):
    return jax.ops.segment_sum(src, seg, n)
kernel_name = 'mk_gnn_preln_d2_gnn_r8_e91151'

def setup_inputs(seed: int=0):
    np.random.seed(seed)
    _w = jnp.asarray

    def _rec_inputs():
        import jax
        import jax.numpy as jnp
        _gk = jax.random.key(seed)
        x = -0.0005121 + 1.001 * jax.random.normal(jax.random.fold_in(_gk, 1), (12500, 32), jnp.float32)
        src = jax.random.randint(jax.random.fold_in(_gk, 2), (200000,), 0, 12500, jnp.int32)
        dst = jnp.minimum((12500 * jax.random.uniform(jax.random.fold_in(_gk, 3), (200000,)) ** 2.0).astype(jnp.int32), 99999)
        _o = jnp.argsort(dst, stable=True)
        src = src[_o]
        dst = dst[_o]
        edge_attr_16 = 0.000254156 + 0.999948 * jax.random.normal(jax.random.fold_in(_gk, 11), (200000, 16), jnp.float32)
        return (x, src, dst, edge_attr_16)
    x, src, dst, edge_attr_16 = _rec_inputs()

    def _L0_gnn_setup():
        import jax, jax.numpy as jnp
        import numpy as np
        N = 12500
        E = 200000
        IN_C = 32
        OUT_C = 32

        def _gcn_norm(edge_index, num_nodes):
            loops = jnp.arange(num_nodes, dtype=edge_index.dtype)
            src = jnp.concatenate([edge_index[0], loops])
            dst = jnp.concatenate([edge_index[1], loops])
            deg = jax.ops.segment_sum(jnp.ones_like(dst, dtype=jnp.float32), dst, num_segments=num_nodes)
            dinv = jnp.where(deg > 0, jax.lax.rsqrt(deg), 0.0)
            norm = dinv[src] * dinv[dst]
            return (src, dst, norm)
        key = jax.random.key(seed)
        k1, k2, k3, k4 = jax.random.split(key, 4)
        x = jax.random.normal(k1, (N, IN_C), dtype=jnp.float32)
        edge_index = jax.random.randint(k2, (2, E), 0, N, dtype=jnp.int64)
        W1 = jax.random.normal(k3, (IN_C, OUT_C), dtype=jnp.float32) * 0.1
        W2 = jax.random.normal(k4, (IN_C, OUT_C), dtype=jnp.float32) * 0.1
        b1 = jnp.zeros((OUT_C,), dtype=jnp.float32)
        b2 = jnp.zeros((OUT_C,), dtype=jnp.float32)
        return {'x': x, 'edge_index': edge_index, 'W1': W1, 'b1': b1, 'W2': W2, 'b2': b2}
    _L0_gnn_all = _L0_gnn_setup()
    _L0_gnn_in = {k: v for k, v in _L0_gnn_all.items() if k in ('W1', 'b1', 'W2', 'b2')}
    del _L0_gnn_all

    def _L1_gnn_setup():
        import jax, jax.numpy as jnp
        import numpy as np
        N_NODES = 6250
        N_EDGES = 100000
        NODE_D, EDGE_D = (32, 16)
        FLOW_IN, FLOW_H, FLOW_OUT = (2 * NODE_D + EDGE_D, 64, 64)
        NODE_H, NODE_OUT = (64, 32)

        def _mlp(h, W1, b1, W2, b2):
            h = jax.nn.relu(h @ W1 + b1)
            return h @ W2 + b2
        key = jax.random.key(seed)
        ks = jax.random.split(key, 8)
        return {'x': jax.random.normal(ks[0], (N_NODES, NODE_D), dtype=jnp.float32), 'edge_index': jax.random.randint(ks[1], (2, N_EDGES), 0, N_NODES, dtype=jnp.int64), 'edge_attr': jax.random.normal(ks[2], (N_EDGES, EDGE_D), dtype=jnp.float32), 'Wf1': jax.random.normal(ks[3], (FLOW_IN, FLOW_H), dtype=jnp.float32) * (1.0 / np.sqrt(FLOW_IN)), 'bf1': jnp.zeros((FLOW_H,), dtype=jnp.float32), 'Wf2': jax.random.normal(ks[4], (FLOW_H, FLOW_OUT), dtype=jnp.float32) * (1.0 / np.sqrt(FLOW_H)), 'bf2': jnp.zeros((FLOW_OUT,), dtype=jnp.float32), 'Wn1': jax.random.normal(ks[5], (FLOW_OUT, NODE_H), dtype=jnp.float32) * (1.0 / np.sqrt(FLOW_OUT)), 'bn1': jnp.zeros((NODE_H,), dtype=jnp.float32), 'Wn2': jax.random.normal(ks[6], (NODE_H, NODE_OUT), dtype=jnp.float32) * (1.0 / np.sqrt(NODE_H)), 'bn2': jnp.zeros((NODE_OUT,), dtype=jnp.float32)}
    _L1_gnn_all = _L1_gnn_setup()
    _L1_gnn_in = {k: v for k, v in _L1_gnn_all.items() if k in ('Wf1', 'bf1', 'Wf2', 'bf2', 'Wn1', 'bn1', 'Wn2', 'bn2')}
    del _L1_gnn_all
    return {'x': x, 'src': src, 'dst': dst, 'edge_attr_16': edge_attr_16, 'L0_gnn_W1': _L0_gnn_in['W1'], 'L0_gnn_b1': _L0_gnn_in['b1'], 'L0_gnn_W2': _L0_gnn_in['W2'], 'L0_gnn_b2': _L0_gnn_in['b2'], 'L1_gnn_Wf1': _L1_gnn_in['Wf1'], 'L1_gnn_bf1': _L1_gnn_in['bf1'], 'L1_gnn_Wf2': _L1_gnn_in['Wf2'], 'L1_gnn_bf2': _L1_gnn_in['bf2'], 'L1_gnn_Wn1': _L1_gnn_in['Wn1'], 'L1_gnn_bn1': _L1_gnn_in['bn1'], 'L1_gnn_Wn2': _L1_gnn_in['Wn2'], 'L1_gnn_bn2': _L1_gnn_in['bn2']}

def reference(x, src, dst, edge_attr_16, L0_gnn_W1, L0_gnn_b1, L0_gnn_W2, L0_gnn_b2, L1_gnn_Wf1, L1_gnn_bf1, L1_gnn_Wf2, L1_gnn_bf2, L1_gnn_Wn1, L1_gnn_bn1, L1_gnn_Wn2, L1_gnn_bn2):
    import jax
    import jax.numpy as jnp

    def _L0_gnn_ref(x, edge_index, W1, b1, W2, b2):
        import jax, jax.numpy as jnp
        import numpy as np
        N = 12500
        E = 200000
        IN_C = 32
        OUT_C = 32

        def _gcn_norm(edge_index, num_nodes):
            loops = jnp.arange(num_nodes, dtype=edge_index.dtype)
            src = jnp.concatenate([edge_index[0], loops])
            dst = jnp.concatenate([edge_index[1], loops])
            deg = jax.ops.segment_sum(jnp.ones_like(dst, dtype=jnp.float32), dst, num_segments=num_nodes)
            dinv = jnp.where(deg > 0, jax.lax.rsqrt(deg), 0.0)
            norm = dinv[src] * dinv[dst]
            return (src, dst, norm)
        src, dst, norm = _gcn_norm(edge_index, N)
        h = x @ (W1 + W2)
        msg = h[src] * norm[:, None]
        agg = jax.ops.segment_sum(msg, dst, num_segments=N)
        return jax.nn.relu(agg + b1 + b2)

    def _L1_gnn_ref(x, edge_index, edge_attr, Wf1, bf1, Wf2, bf2, Wn1, bn1, Wn2, bn2):
        import jax, jax.numpy as jnp
        import numpy as np
        N_NODES = 6250
        N_EDGES = 100000
        NODE_D, EDGE_D = (32, 16)
        FLOW_IN, FLOW_H, FLOW_OUT = (2 * NODE_D + EDGE_D, 64, 64)
        NODE_H, NODE_OUT = (64, 32)

        def _mlp(h, W1, b1, W2, b2):
            h = jax.nn.relu(h @ W1 + b1)
            return h @ W2 + b2
        past, future = (edge_index[0], edge_index[1])
        x_p = x[past]
        x_f = x[future]
        flow_fwd = jnp.concatenate([x_f, x_p, edge_attr], axis=1)
        flow_bwd = jnp.concatenate([x_p, x_f, edge_attr], axis=1)
        flow_total_in = jnp.concatenate([flow_fwd, flow_bwd], axis=0)
        flow_processed = _mlp(flow_total_in, Wf1, bf1, Wf2, bf2)
        dest = jnp.concatenate([future, past], axis=0)
        flow_total = jax.ops.segment_sum(flow_processed, dest, num_segments=x.shape[0])
        return _mlp(flow_total, Wn1, bn1, Wn2, bn2)
    edge_index = jnp.stack([src, dst])
    h = jnp.maximum(_layernorm(x, axis=-1), 0.0)
    x = x + _L0_gnn_ref(h, edge_index, L0_gnn_W1, L0_gnn_b1, L0_gnn_W2, L0_gnn_b2)
    h = jnp.maximum(_layernorm(x, axis=-1), 0.0)
    x = x + _L1_gnn_ref(h, edge_index, edge_attr_16, L1_gnn_Wf1, L1_gnn_bf1, L1_gnn_Wf2, L1_gnn_bf2, L1_gnn_Wn1, L1_gnn_bn1, L1_gnn_Wn2, L1_gnn_bn2)
    return x

_drawn_inputs = setup_inputs


def setup_inputs(seed=0):
    import zlib

    import numpy as np

    out = dict(_drawn_inputs(seed))
    spreads = {'L0_gnn_b1': (0.0, 0.1),
     'L0_gnn_b2': (0.0, 0.1),
     'L1_gnn_bf1': (0.0, 0.1),
     'L1_gnn_bf2': (0.0, 0.1),
     'L1_gnn_bn1': (0.0, 0.8),
     'L1_gnn_bn2': (0.0, 0.8)}
    factors = {}
    for name, (base, spread) in spreads.items():
        noise = np.random.default_rng([zlib.crc32(name.encode()), seed]).standard_normal(out[name].shape)
        drawn = base * np.exp(spread * noise) if base else spread * noise
        out[name] = jnp.asarray(drawn.astype(out[name].dtype))
    for name, factor in factors.items():
        out[name] = (out[name] * factor).astype(out[name].dtype)
    return out
```

```python
import concourse.bass as bass
from concourse import mybir
from contextlib import ExitStack

N, E = 12500, 200000
D, ED, H = 32, 16, 64
P = 128
NB = -(-N // P)
T = -(-E // P)
GB = 4
NG = -(-(NB + 1) // GB)
NBP = NG * GB
NR = NBP * P
TRASH = NB * P
TC = -(-T // P)
TW = TC * P
RING = 4
NPS = 2
GX = 2
C2 = 2 * H
CX = H + 1
BIG = 1.0e6
EPS = 1e-5


def done(j):
    return j + 1 + RING


def freed(j, depth):
    return j + 1 + RING - depth


def build(nc, x, src, dst, ea, W1, b1, W2, b2, Wf1, bf1, Wf2, bf2, Wn1, bn1, Wn2, bn2, out):
    fp32, bf16, i32 = mybir.dt.float32, mybir.dt.bfloat16, mybir.dt.int32
    ALU = mybir.AluOpType
    ACT = mybir.ActivationFunctionType
    AXX = mybir.AxisListType.X
    ds = bass.ds

    g_tab = nc.dram_tensor("g_tab", (NR, D), fp32, kind="Internal").ap()
    ba_tab = nc.dram_tensor("ba_tab", (NR, C2), fp32, kind="Internal").ap()
    sum_tab = [nc.dram_tensor(f"sum_tab{k}", (NR, CX), fp32, kind="Internal").ap() for k in range(2 * GX)]

    ctx = ExitStack()
    with ctx:
        def sb(name, shape, dt=fp32):
            return ctx.enter_context(nc.sbuf_tensor(name, shape, dt))[:, :]

        def ps(name, shape, dt=fp32):
            return ctx.enter_context(nc.psum_tensor(name, shape, dt))[:, :]

        def sem(name):
            return ctx.enter_context(nc.semaphore(name))

        ctx.enter_context(nc.allow_non_contiguous_dma(reason="a bias as a column"))

        LENT = NBP * D
        x_sb = sb("x_sb", [P, LENT])
        xc = sb("xc", [P, LENT])
        gs = sb("gs", [P, LENT])
        hx = sb("hx", [P, LENT])
        acc = sb("acc", [P, NBP * CX])
        agg = sb("agg", [P, NBP * D])
        srci = sb("srci", [P, TW], i32)
        dsti = sb("dsti", [P, TW], i32)
        srcf = sb("srcf", [P, TW])
        dstf = sb("dstf", [P, TW])
        hif = sb("hif", [P, TW])
        srcH = sb("srcH", [P, TW], bf16)
        srcL = sb("srcL", [P, TW], bf16)
        lof = hx[:, 0:TW]
        dup = xc[:, 0:TW]
        tmp_i = xc[:, 0:TW].bitcast(i32)
        tminb = x_sb[:, 0:TW]
        tmaxb = gs[:, 0:TW]
        assert TW <= LENT

        iota_i = sb("iota_i", [P, P], i32)
        iota_f = sb("iota_f", [P, P])
        iota_b = sb("iota_b", [P, P], bf16)
        chan_i = sb("chan_i", [P, 1], i32)
        chan_f = sb("chan_f", [P, 1])
        trash_f = sb("trash_f", [P, 1])
        zb = sb("zb", [P, P], bf16)
        bnd_i = sb("bnd_i", [P, 4], i32)
        tile_iota = agg[:, 0:TW].bitcast(i32)
        ident = sb("ident", [P, P])
        before = sb("before", [P, P])
        ones = sb("ones", [P, 1])
        negblk = sb("negblk", [P, NB])
        bounds = sb("bounds", [P, 8])
        ptab = sb("ptab", [1, 2 * P])
        pint = sb("pint", [1, 2 * P + 4], i32)
        hist = sb("hist", [P, NBP])
        dinv = sb("dinv", [P, NBP])
        stat = sb("stat", [P, 3 * NBP])
        W12 = sb("W12", [P, 2 * P])
        WBA = sb("WBA", [P, GB * C2])
        WE = sb("WE", [2 * ED, 2 * C2])
        biasr = sb("biasr", [P, C2])
        b12 = sb("b12", [P, 2 * D])
        bn2r = sb("bn2r", [P, D])
        wf2x = sb("wf2x", [CX, H])
        wn1 = sb("wn1", [H, H])
        wn2 = sb("wn2", [H, D])
        bn1c = sb("bn1c", [H, 1])

        oh = sb("oh", [P, 2 * P])
        ohT = sb("ohT", [P, 2 * P])
        same = sb("same", [P, 2 * P])
        ea_at = sb("ea_at", [2 * ED, P])
        ea_in = sb("ea_in", [2 * ED, RING * P])
        ohb = sb("ohb", [P, 8 * 2 * P], bf16)
        identb = sb("identb", [P, P], bf16)
        gat = sb("gat", [P, RING * 2 * C2])
        pre = sb("pre", [P, NPS * 2 * C2])
        msg = sb("msg", [P, NPS * 2 * (C2 + 1)])
        comb = sb("comb", [P, RING * 2 * CX])
        valid = sb("valid", [P, RING * 2])
        gidx = sb("gidx", [P, RING * 2], i32)
        sidx = sb("sidx", [P, RING * 2], i32)
        tdst = sb("tdst", [P, 4 * C2])

        psS = ps("psS", [P, 512])
        psOT = ps("psOT", [P, 1024])
        psO, psT = psOT[:, 0:512], psOT[:, 512:1024]
        psP = ps("psP", [P, 512])
        psC = ps("psC", [P, 512])
        psF = ps("psF", [P, 512])
        psM = ps("psM", [P, 1024])

        in_dma, w_dma, zero_dma, ea_dma = sem("in_dma"), sem("w_dma"), sem("zero_dma"), sem("ea_dma")
        const = sem("const")
        dch = sem("dch")
        tabs_f = sem("tabs_f")
        tile_t = sem("tile_t")
        tile_r = sem("tile_r")
        tile_v = sem("tile_v")
        tile_c = sem("tile_c")
        dve_step, pe_step, act_step = sem("dve_step"), sem("pe_step"), sem("act_step")
        ptab_ready = sem("ptab_ready")
        hoh, hmm, hdone = sem("hoh"), sem("hmm"), sem("hdone")
        sq, sqd = sem("sq"), sem("sqd")
        h_ready, nT, nTs, nM, nE = sem("h_ready"), sem("nT"), sem("nTs"), sem("nM"), sem("nE")
        tab_dma = sem("tab_dma")
        tab_ready = sem("tab_ready")
        gdma = [sem(f"gdma{s}") for s in range(2 * RING)]
        turn = sem("turn")
        gidx0, gath0, oh0, srcT0, same0, mm0, dup0, dupc0, blk0, acc0 = [
            sem(n) for n in ("gidx0", "gath0", "oh0", "srcT0", "same0", "mm0", "dup0", "dupc0", "blk0", "acc0")]
        gdma1 = [sem(f"gdma1_{s}") for s in range(2 * RING)]
        sdma = [sem(f"sdma{s}") for s in range(2 * RING)]
        idx_dma, gidx1, eain1, gath1, tdst_dma, tdst1 = sem("idx_dma"), sem("gidx1"), sem("eain1"), sem("gath1"), sem("tdst_dma"), sem("tdst1")
        valid1, oh1, ohb1, srcT1, same1, ohTp1, ohTs1, pre1, sum1, msg1, comb1, fwd1, combs1, scat1, blk1, acc1, ea1 = [
            sem(n) for n in ("valid1", "oh1", "ohb1", "srcT1", "same1", "ohTp1", "ohTs1", "pre1", "sum1", "msg1",
                             "comb1", "fwd1", "combs1", "scat1", "blk1", "acc1", "ea1")]
        scat_all = sem("scat_all")
        fin_dma = [sem("fin_dma0"), sem("fin_dma1")]
        fsum, fT, fS, fF, fFs, fH, fHs, fO, fOut, out_dma = [
            sem(n) for n in ("fsum", "fT", "fS", "fF", "fFs", "fH", "fHs", "fO", "fOut", "out_dma")]
        sidx_ready = sem("sidx_ready")

        def col(ap, c, n=1):
            return ap[:, ds(c, n)]

        def slot(ap, j, k, w):
            return ap[:, ds((j % RING) * (2 * w) + k * w, w)]

        BASE, FIRST = 2, P + 4

        def pairs_of_block(eng, b):
            s = eng.value_load(pint[0:1, ds(b + BASE, 1)], min_val=0, max_val=NB * (TW // 2))
            e = eng.value_load(pint[0:1, ds(b + BASE + 1, 1)], min_val=0, max_val=NB * (TW // 2) + RING)
            f = eng.value_load(pint[0:1, ds(b + FIRST, 1)], min_val=0, max_val=T)
            return s, e, f

        def first_tile(eng, j, s, f):
            return eng.snap(nc.s_assert_within((j - s) * 2 + f, 0, TW - 2, skip_runtime_bounds_check_because=
                                               "a block's pairs end at its last tile, or RING pairs behind it"))

        def rounds_but_one(eng):
            return eng.value_load(pint[0:1, BASE + NB + 1:BASE + NB + 2], min_val=2, max_val=NB * TW)

        block = ctx.enter_context(nc.Block())

        @block.sync
        def _(sp):
            sp.dma_start(dsti[:, :], dst).then_inc(in_dma, 16)
            sp.dma_start(srci[:, :], src).then_inc(in_dma, 16)
            sp.wait_ge(const, 5)
            for k in range(GB):
                rows = slice(k * D, (k + 1) * D)
                sp.dma_start(W12[rows, k * D:(k + 1) * D], W1).then_inc(w_dma, 16)
                sp.dma_start(W12[rows, P + k * D:P + (k + 1) * D], W2).then_inc(w_dma, 16)
                sp.dma_start(WBA[rows, k * C2:k * C2 + H], Wf1[D:2 * D, :]).then_inc(w_dma, 16)
                sp.dma_start(WBA[rows, k * C2 + H:(k + 1) * C2], Wf1[0:D, :]).then_inc(w_dma, 16)
            for k in range(2):
                rows = slice(k * ED, (k + 1) * ED)
                sp.dma_start(WE[rows, k * C2:k * C2 + H], Wf1[2 * D:, :]).then_inc(w_dma, 16)
                sp.dma_start(WE[rows, k * C2 + H:(k + 1) * C2], Wf1[2 * D:, :]).then_inc(w_dma, 16)
            row = lambda v, n: v.rearrange("(a n) -> a n", a=1).to_broadcast([P, n])
            sp.dma_start(biasr[:, H:C2], row(bf1, H)).then_inc(w_dma, 16)
            sp.dma_start(b12[:, 0:D], row(b1, D)).then_inc(w_dma, 16)
            sp.dma_start(b12[:, D:2 * D], row(b2, D)).then_inc(w_dma, 16)
            sp.dma_start(bn2r[:, :], row(bn2, D)).then_inc(w_dma, 16)
            sp.dma_start(wf2x[0:H, :], Wf2).then_inc(w_dma, 16)
            sp.dma_start(wf2x[H:CX, :], bf2.rearrange("(a n) -> a n", a=1)).then_inc(w_dma, 16)
            sp.dma_start(wn1[:, :], Wn1).then_inc(w_dma, 16)
            sp.dma_start(wn2[:, :], Wn2).then_inc(w_dma, 16)
            sp.dma_start(bn1c[:, :], bn1.rearrange("(n a) -> n a", a=1)).then_inc(w_dma, 16)
            for k in range(2 * GX):
                sp.dma_start(sum_tab[k].rearrange("(p b) c -> p (b c)", p=P), acc[:, :]).then_inc(zero_dma, 16)
            sp.wait_ge(ptab_ready, 1)
            sp.dma_start(x_sb, x).then_inc(in_dma, 16)

            g_view = g_tab.rearrange("(b p) c -> p b c", p=P)
            sp.sem_inc(tab_ready, 1)
            sp.wait_ge(nE, NG + 2)
            sp.dma_start(g_view, gs.rearrange("p (b c) -> p b c", c=D)).then_inc(tab_dma, 16)
            sp.wait_ge(tab_dma, 16)
            sp.sem_inc(tab_ready, 1)

            ba_view = ba_tab.rearrange("(q b p) c -> q p b c", p=P, b=GB)
            for q in range(NG):
                sp.wait_ge(nE, NG + q + 3)
                sp.dma_start(ba_view[q, :, :, :], gat[:, (q % 2) * 512:(q % 2) * 512 + 512]
                             .rearrange("p (b c) -> p b c", c=C2)).then_inc(tab_dma, 16)
                sp.wait_ge(tab_dma, 16 * (q + 2))
                sp.sem_inc(tab_ready, 1)
            def load_block(b, nth):
                rows = ba_tab[ds(b * P, P), :]
                at = (b % 4) * C2
                sp.dma_start(tdst[:, ds(at, H)], rows[:, H:C2]).then_inc(tdst_dma, 16)
                sp.dma_start(tdst[:, ds(at + H, H)], rows[:, 0:H]).then_inc(tdst_dma, 16)
                sp.wait_ge(tdst_dma, nth * 32)
                sp.sem_inc(tdst1, 1)

            sp.sem_inc(gidx1, RING)
            sp.sem_inc(eain1, RING)
            load_block(0, 1)
            with sp.Fori(0, NB) as b:
                s, e, f = pairs_of_block(sp, b)
                old = sp.value_load(pint[0:1, ds(b + BASE - 2, 1)], min_val=0, max_val=NB * (TW // 2))
                sp.wait_ge(pre1, old + RING)
                load_block(b + 1, b + 2)
                with sp.Fori(s, e) as j:
                    t = first_tile(sp, j, s, f)
                    sp.wait_ge(gath1, freed(j, RING))
                    sp.dma_start(gidx[:, ds((j % RING) * 2, 2)],
                                 col(srci, t, 2)).then_inc(idx_dma, 16)
                    sp.wait_ge(ea1, freed(j, RING))
                    sp.dma_start(ea_in[:, ds((j % RING) * P, P)], ea[ds(t * ED, 2 * ED), :]).then_inc(ea_dma, 16)
                    sp.wait_ge(idx_dma, j * 16 + 16)
                    sp.sem_inc(gidx1, 1)
                    sp.wait_ge(ea_dma, j * 16 + 16)
                    sp.sem_inc(eain1, 1)

            sp.wait_ge(scat_all, 1)
            for q in range(NG):
                if q >= 2:
                    sp.wait_ge(fsum, q - 1)
                for k in range(2 * GX):
                    at = ((q % 2) * 2 * GX + k) * GB * CX
                    sp.dma_start(hx[:, at:at + GB * CX].rearrange("p (b c) -> p b c", c=CX),
                                 sum_tab[k].rearrange("(q b p) c -> q p b c", p=P, b=GB)[q, :, :, :])\
                      .then_inc(fin_dma[q % 2], 16)
                if q >= 1:
                    sp.wait_ge(fOut, q)
                    sp.dma_start(out[:, (q - 1) * GB * D:q * GB * D],
                                 xc[:, ((q - 1) % 2) * GB * D:((q - 1) % 2 + 1) * GB * D]).then_inc(out_dma, 16)
            sp.wait_ge(fOut, NG)
            sp.dma_start(out[:, (NG - 1) * GB * D:NG * GB * D],
                         xc[:, ((NG - 1) % 2) * GB * D:((NG - 1) % 2 + 1) * GB * D]).then_inc(out_dma, 16)
            sp.wait_ge(out_dma, 16 * NG)

        @block.gpsimd
        def _(pool):
            nc.gpsimd.memset(W12[:, :], 0.0).then_inc(const, 1)
            nc.gpsimd.memset(WBA[:, :], 0.0).then_inc(const, 1)
            nc.gpsimd.memset(WE[:, :], 0.0).then_inc(const, 1)
            nc.gpsimd.memset(biasr[:, :], 0.0).then_inc(const, 1)
            nc.gpsimd.memset(acc[:, :], 0.0).then_inc(const, 1)
            nc.gpsimd.iota(iota_i[:, :], pattern=[[1, P]], base=0, channel_multiplier=0).then_inc(const, 1)
            nc.gpsimd.memset(ident[:, :], 0.0).then_inc(const, 1)
            nc.gpsimd.memset(before[:, :], 0.0).then_inc(const, 1)
            nc.gpsimd.memset(ones[:, :], 1.0).then_inc(const, 1)
            nc.gpsimd.memset(msg[:, :], 1.0).then_inc(const, 1)
            nc.gpsimd.memset(zb[:, :], 0.0).then_inc(const, 1)
            pool.wait_ge(const, 11)
            nc.gpsimd.affine_select(out=ident[:, :], in_=ident[:, :], compare_op=ALU.not_equal, fill=1.0,
                                    base=0, pattern=[[-1, P]], channel_multiplier=1).then_inc(const, 1)
            nc.gpsimd.affine_select(out=before[:, :], in_=before[:, :], compare_op=ALU.is_ge, fill=1.0,
                                    base=0, pattern=[[-1, P]], channel_multiplier=1).then_inc(const, 1)
            nc.gpsimd.iota(chan_i[:, :], pattern=[[0, 1]], base=0, channel_multiplier=1).then_inc(const, 1)
            nc.gpsimd.iota(tile_iota, pattern=[[1, TW]], base=1, channel_multiplier=0).then_inc(const, 1)

            def gathers(v, table, width, sems):
                for k in range(2):
                    s = 2 * v + k
                    pool.indirect_dma_start(gat[:, s * C2:s * C2 + width], None, table,
                                            bass.IndirectOffsetOnAxis(ap=gidx[:, s:s + 1], axis=0))\
                        .then_inc(sems[s], 16)

            def landed(sems, v, turns):
                pool.wait_ge(sems[2 * v], turns * 16)
                pool.wait_ge(sems[2 * v + 1], turns * 16)

            def step0(r, v, first):
                j = r * RING + v
                if not first or v >= 2:
                    landed(gdma, (v - 2) % RING, r + 1 if v >= 2 else r)
                    pool.sem_inc(gath0, 1)
                pool.wait_ge(gidx0, done(j))
                pool.wait_ge(mm0, freed(j, RING))
                pool.sem_inc(turn, 1)
                gathers(v, g_tab, D, gdma)

            pool.sem_inc(gath0, RING)
            pool.sem_inc(gath1, RING)
            pool.sem_inc(scat1, RING)
            pool.wait_ge(ptab_ready, 1)
            last = rounds_but_one(pool)
            pool.wait_ge(tab_ready, 2)
            for v in range(RING):
                step0(0, v, True)
            with pool.Fori(1, last + 1) as r:
                for v in range(RING):
                    step0(r, v, False)
            for v in (2, 3):
                landed(gdma, v, last + 1)
                pool.sem_inc(gath0, 1)

            def scatter(v, before_r, first):
                pool.wait_ge(combs1, (before_r + 2) * RING + v + 1)
                if not first:
                    landed(sdma, (v - GX) % RING, before_r + 2 if v >= GX else before_r + 1)
                    pool.sem_inc(scat1, 1)
                else:
                    pool.sem_inc(turn, 1)
                for k in range(2):
                    s = 2 * v + k
                    pool.indirect_dma_start(sum_tab[(v % GX) * 2 + k],
                                            bass.IndirectOffsetOnAxis(ap=sidx[:, s:s + 1], axis=0),
                                            comb[:, s * CX:(s + 1) * CX], None,
                                            compute_op=ALU.add).then_inc(sdma[s], 16)

            def step1(before_r, v, gather_only, first):
                if not gather_only or v >= 1:
                    landed(gdma1, (v - 1) % RING, before_r + 2 if v >= 1 else before_r + 1)
                    pool.sem_inc(gath1, 1)
                j = (before_r + 1) * RING + v
                pool.wait_ge(gidx1, done(j))
                pool.wait_ge(sum1, freed(j, RING))
                pool.sem_inc(turn, 1)
                gathers(v, ba_tab, C2, gdma1)
                if v >= 3:
                    scatter(v - 3, before_r, first)
                elif not gather_only:
                    scatter((v - 3) % RING, before_r - 1, first and v == 0)

            pool.wait_ge(zero_dma, 16 * 2 * GX)
            pool.wait_ge(sidx_ready, 1)
            for r in range(2):
                for v in range(RING):
                    step1(r - 1, v, r == 0, r == 0 or v == 0)
            with pool.Fori(1, last) as before_r:
                for v in range(RING):
                    step1(before_r, v, False, False)
            landed(gdma1, RING - 1, last + 1)
            pool.sem_inc(gath1, 1)
            for v in range(1, RING):
                scatter(v, last - 1, False)
            for v in range(RING):
                landed(sdma, v, last + 1)
            pool.sem_inc(scat_all, 1)

        @block.scalar
        def _(act):
            act.preload_act_table(ACT.Sqrt)

            def square_root(n, ap):
                act.wait_ge(sq, n)
                nc.scalar.activation(ap, ap, ACT.Sqrt).then_inc(sqd, 1)

            def node_groups(n0):
                with act.Fori(0, NG) as q:
                    act.wait_ge(nT, q + (n0 + 1))
                    act.wait_ge(nM, q + (n0 + 1))
                    act.sem_inc(act_step, 1)
                    nc.scalar.activation(ohT[:, ds((q % 2) * P, P)], psOT[:, ds((q % 2) * 512, P)], ACT.Copy)\
                        .then_inc(nTs, 1)

            square_root(1, dinv[:, :])
            square_root(2, stat[:, 2 * NBP:3 * NBP])
            act.preload_act_table(ACT.Copy)
            act.sem_inc(nTs, 2)
            node_groups(0)

            act.sem_inc(gidx0, RING)
            with act.Fori(0, NB) as b:
                s, e, f = pairs_of_block(act, b)
                with act.Fori(s, e) as j:
                    t = first_tile(act, j, s, f)
                    act.wait_ge(gath0, freed(j, RING))
                    act.sem_inc(act_step, 1)
                    nc.scalar.activation(gidx[:, ds((j % RING) * 2, 2)], col(srci, t, 2), ACT.Copy)\
                        .then_inc(gidx0, 1)

            act.preload_act_table(ACT.Sqrt)
            square_root(3, stat[:, 2 * NBP:3 * NBP])
            act.preload_act_table(ACT.Copy)
            node_groups(NG)

            act.sem_inc(ohTs1, RING)
            act.sem_inc(ea1, RING)
            act.sem_inc(acc1, 1)
            act.sem_inc(msg1, RING)
            act.sem_inc(combs1, RING)
            act.wait_ge(sidx_ready, 1)
            act.preload_act_table(ACT.Relu)
            with act.Fori(0, NB) as b:
                s, e, f = pairs_of_block(act, b)
                with act.Fori(s, e) as j:
                    t = first_tile(act, j, s, f)
                    act.wait_ge(eain1, done(j))
                    act.wait_ge(pre1, freed(j, 1))
                    act.sem_inc(act_step, 1)
                    nc.scalar.activation(ea_at[:, :], ea_in[:, ds((j % RING) * P, P)], ACT.Copy).then_inc(ea1, 1)
                    act.wait_ge(ohTp1, done(j))
                    act.sem_inc(act_step, 1)
                    nc.scalar.activation(ohT[:, :], psO[:, 0:2 * P], ACT.Copy).then_inc(ohTs1, 1)
                    act.wait_ge(sum1, done(j))
                    act.wait_ge(fwd1, freed(j, NPS))
                    act.sem_inc(act_step, 1)
                    nc.scalar.activation(
                        msg[:, ds((j % NPS) * 2 * (C2 + 1), 2 * (C2 + 1))].rearrange("p (k c) -> p k c", k=2)[:, :, 0:C2],
                        pre[:, ds((j % NPS) * 2 * C2, 2 * C2)].rearrange("p (k c) -> p k c", k=2), ACT.Relu)\
                        .then_inc(msg1, 1)
                    act.wait_ge(scat1, freed(j, RING))
                    act.sem_inc(act_step, 1)
                    nc.scalar.activation(sidx[:, ds((j % RING) * 2, 2)], col(dsti, t, 2), ACT.Copy)
                    act.wait_ge(comb1, done(j))
                    act.sem_inc(act_step, 1)
                    nc.scalar.activation(comb[:, ds((j % RING) * 2 * CX, 2 * CX)], psC[:, 0:2 * CX],
                                         ACT.Copy).then_inc(combs1, 1)
                act.wait_ge(blk1, b + 1)
                act.sem_inc(act_step, 1)
                nc.scalar.activation(acc[:, ds(b * CX, H)], psF[:, 0:H], ACT.Copy).then_inc(acc1, 1)

            for q in range(NG):
                act.wait_ge(fT, q + 1)
                nc.scalar.activation(pre[0:CX, :], psT[0:CX, :], ACT.Copy).then_inc(fS, 1)
                act.wait_ge(fF, q + 1)
                nc.scalar.activation(gat[0:H, 0:512], psM[0:H, 0:512], ACT.Copy).then_inc(fFs, 1)
                act.wait_ge(fH, q + 1)
                nc.scalar.activation(gat[0:H, 512:1024], psP[0:H, :], ACT.Relu, bias=bn1c[:, :]).then_inc(fHs, 1)

        @block.vector
        def _(dve):
            chain = [0]

            def link(ins):
                chain[0] += 1
                ins.then_inc(dch, 1)
                dve.wait_ge(dch, chain[0])

            V = nc.vector
            dve.wait_ge(const, 15)
            V.tensor_copy(iota_f[:, :], iota_i[:, :])
            V.tensor_copy(iota_b[:, :], iota_i[:, :])
            V.tensor_copy(identb[:, :], ident[:, :])
            link(V.tensor_copy(chan_f[:, :], chan_i[:, :]))
            V.tensor_scalar(trash_f[:, :], chan_f[:, :], float(TRASH), None, ALU.add)
            link(V.tensor_scalar(negblk[:, :], iota_f[:, 0:NB], float(-P), None, ALU.mult))
            dve.wait_ge(in_dma, 32)
            V.tensor_copy(srcf[:, :], srci[:, :])
            V.tensor_copy(dstf[:, :], dsti[:, :])
            link(V.tensor_scalar(tmp_i, dsti[:, :], 7, None, ALU.arith_shift_right))
            link(V.tensor_copy(hif[:, :], tmp_i))
            link(V.tensor_scalar(tmp_i, srci[:, :], P - 1, None, ALU.bitwise_and))
            link(V.tensor_copy(srcL[:, :], tmp_i))
            link(V.tensor_tensor(srcH[:, :], srcf[:, :], srcL[:, :], ALU.subtract))
            link(V.tensor_scalar(tmp_i, dsti[:, :], P - 1, None, ALU.bitwise_and))
            V.tensor_copy(lof, tmp_i).then_inc(tabs_f, 1)
            dve.wait_ge(tabs_f, 1)

            with dve.Fori(0, TC) as c:
                dve.wait_ge(tile_t, c * 3 + 1)
                V.tensor_reduce(bounds[:, 1:2], psS[:, 0:P], axis=AXX, op=ALU.max)
                V.tensor_scalar(same[:, 0:P], psS[:, 0:P], 0.0, BIG, ALU.is_lt, ALU.mult).then_inc(tile_v, 1)
                dve.wait_ge(tile_v, c * 2 + 1)
                V.tensor_tensor(same[:, P:2 * P], psS[:, 0:P], same[:, 0:P], ALU.add).then_inc(tile_v, 1)
                dve.wait_ge(tile_v, c * 2 + 2)
                V.tensor_reduce(bounds[:, 0:1], same[:, P:2 * P], axis=AXX, op=ALU.min).then_inc(tile_r, 1)
                dve.wait_ge(tile_t, c * 3 + 3)
                dve.sem_inc(dve_step, 1)
                V.tensor_copy(tminb[:, ds(c * P, P)], psS[:, P:2 * P])
                V.tensor_copy(tmaxb[:, ds(c * P, P)], psS[:, 2 * P:3 * P]).then_inc(tile_c, 1)
            dve.wait_ge(tile_c, TC + 1)
            link(V.tensor_scalar(bounds[:, 2:3], chan_f[:, :], float(P), None, ALU.mult))
            link(V.tensor_scalar(bounds[:, 3:4], bounds[:, 2:3], float(P - 1), None, ALU.add))
            link(V.tensor_scalar(tminb, tminb, bounds[:, 3:4], None, ALU.is_le))
            link(V.tensor_scalar(tmaxb, tmaxb, bounds[:, 2:3], None, ALU.is_ge))
            link(V.tensor_tensor(tminb, tminb, tmaxb, ALU.mult))
            link(V.tensor_copy(tmaxb, tile_iota))
            link(V.tensor_tensor(tmaxb, tmaxb, tminb, ALU.mult))
            link(V.tensor_reduce(bounds[:, 1:2], tmaxb, axis=AXX, op=ALU.max))
            link(V.tensor_scalar(tminb, tminb, -BIG, None, ALU.mult))
            link(V.tensor_tensor(tmaxb, tmaxb, tminb, ALU.add))
            link(V.tensor_reduce(bounds[:, 0:1], tmaxb, axis=AXX, op=ALU.min))
            link(V.tensor_scalar(bounds[:, 0:1], bounds[:, 0:1], BIG - 1.0, None, ALU.add))
            link(V.tensor_scalar(bounds[:, 4:5], bounds[:, 1:2], 1.0, -1.0, ALU.max, ALU.add))
            link(V.tensor_tensor(bounds[:, 0:1], bounds[:, 0:1], bounds[:, 4:5], ALU.min))
            link(V.tensor_tensor(bounds[:, 5:6], bounds[:, 4:5], bounds[:, 0:1], ALU.subtract))
            link(V.tensor_copy(bnd_i[:, 0:1], bounds[:, 5:6]))
            link(V.tensor_scalar(bnd_i[:, 1:2], bnd_i[:, 0:1], 1, None, ALU.arith_shift_right))
            link(V.tensor_copy(bounds[:, 6:7], bnd_i[:, 1:2]))
            V.tensor_scalar(bounds[:, 7:8], bounds[:, 6:7], 1.0, None, ALU.add).then_inc(tile_r, 1)
            dve.wait_ge(tile_t, 3 * TC + 2)
            link(V.memset(pint[:, :], 0))
            link(V.tensor_copy(ptab[0:1, 0:2 * P], psS[0:1, 0:2 * P]))
            V.tensor_copy(pint[0:1, BASE:BASE + NB], ptab[0:1, 0:NB])
            V.tensor_copy(pint[0:1, FIRST:FIRST + NB], ptab[0:1, P:P + NB])
            link(V.tensor_scalar(ptab[0:1, NB:NB + 1], ptab[0:1, NB:NB + 1], float(RING - 1), None, ALU.add))
            link(V.tensor_copy(bnd_i[0:1, 2:3], ptab[0:1, NB:NB + 1]))
            link(V.tensor_scalar(bnd_i[0:1, 3:4], bnd_i[0:1, 2:3], 2, None, ALU.arith_shift_right))
            link(V.tensor_scalar(bnd_i[0:1, 2:3], bnd_i[0:1, 3:4], 2, None, ALU.logical_shift_left))
            link(V.tensor_copy(pint[0:1, BASE + NB:BASE + NB + 1], bnd_i[0:1, 2:3]))
            V.tensor_scalar(pint[0:1, BASE + NB + 1:BASE + NB + 2], bnd_i[0:1, 3:4], -1.0, None, ALU.add)\
                .then_inc(ptab_ready, 1)

            with dve.Fori(0, (T + 3) // 4) as i:
                for u in range(4):
                    at = ((i % 2) * 4 + u) * 2 * P
                    if u == 0:
                        dve.wait_ge(hmm, i + 1)
                    V.tensor_scalar(ohb[:, ds(at, P)], iota_b[:, :], col(lof, i * 4 + u), None, ALU.is_equal)
                    ins = V.tensor_scalar(ohb[:, ds(at + P, NB)], iota_b[:, 0:NB], col(hif, i * 4 + u), None,
                                          ALU.is_equal)
                ins.then_inc(hoh, 1)
            dve.wait_ge(hdone, 1)
            link(V.memset(hist[:, :], 0.0))
            link(V.memset(agg[:, :], 0.0))
            link(V.tensor_copy(hist[:, 0:NB], psO[:, 0:NB]))
            V.tensor_scalar(dinv[:, :], hist[:, :], 1.0, None, ALU.add).then_inc(sq, 1)
            dve.wait_ge(sqd, 1)
            link(V.reciprocal(dinv[:, :], dinv[:, :]))

            def blocks(ap, c=D):
                return ap.rearrange("p (b c) -> p b c", c=c)

            def spread(ap, n=NBP):
                return ap.rearrange("p (b a) -> p b a", a=1).to_broadcast([P, n, D])

            def layernorm_relu(xin, centred, tmp, n):
                mean, var = stat[:, 0:NBP], stat[:, 2 * NBP:3 * NBP]
                link(V.tensor_reduce(mean, blocks(xin), axis=AXX, op=ALU.add))
                link(V.tensor_scalar(mean, mean, 1.0 / D, None, ALU.mult))
                link(V.tensor_tensor(blocks(centred), blocks(xin), spread(mean), ALU.subtract))
                link(V.tensor_tensor(tmp, centred, centred, ALU.mult))
                link(V.tensor_reduce(var, blocks(tmp), axis=AXX, op=ALU.add))
                V.tensor_scalar(var, var, 1.0 / D, EPS, ALU.mult, ALU.add).then_inc(sq, 1)
                dve.wait_ge(sqd, n)
                link(V.reciprocal(var, var))
                V.scalar_tensor_tensor(out=blocks(centred), in0=blocks(centred), scalar=0.0, in1=spread(var),
                                       op0=ALU.max, op1=ALU.mult).then_inc(h_ready, 1)

            dve.wait_ge(in_dma, 48)
            dve.wait_ge(w_dma, 16 * (4 * GB + 4 + 9))
            link(V.tensor_tensor(W12[:, 0:P], W12[:, 0:P], W12[:, P:2 * P], ALU.add))
            link(V.tensor_tensor(b12[:, 0:D], b12[:, 0:D], b12[:, D:2 * D], ALU.add))
            dve.sem_inc(nE, 2)
            layernorm_relu(x_sb, hx, xc, 2)
            with dve.Fori(0, NG) as q:
                dve.wait_ge(nM, q + 3)
                V.tensor_tensor(blocks(gs[:, ds(q * P, P)]), blocks(psM[:, ds((q % 2) * 512, P)]),
                                dinv[:, ds(q * GB, GB)].rearrange("p (b a) -> p b a", a=1).to_broadcast([P, GB, D]),
                                ALU.mult).then_inc(nE, 1)

            link(V.memset(dup, 0.0))
            dve.sem_inc(oh0, RING)
            dve.sem_inc(same0, RING)
            dve.sem_inc(dupc0, RING)
            dve.sem_inc(acc0, 1)
            with dve.Fori(0, NB) as b:
                s, e, f = pairs_of_block(dve, b)
                with dve.Fori(s, e) as j:
                    t = first_tile(dve, j, s, f)
                    dve.wait_ge(mm0, freed(j, 1))
                    for k in range(2):
                        ins = V.tensor_scalar(oh[:, k * P:(k + 1) * P], iota_f[:, :], col(dstf, t + k),
                                              col(negblk, b), ALU.subtract, ALU.is_equal)
                    ins.then_inc(oh0, 1)
                    dve.wait_ge(srcT0, done(j))
                    dve.wait_ge(dup0, freed(j, 1))
                    for k in range(2):
                        ins = V.scalar_tensor_tensor(out=same[:, k * P:(k + 1) * P], in0=psS[:, k * P:(k + 1) * P],
                                                     scalar=col(srcf, t + k), in1=before[:, :],
                                                     op0=ALU.is_equal, op1=ALU.mult)
                    ins.then_inc(same0, 1)
                    dve.wait_ge(dup0, done(j))
                    dve.sem_inc(dve_step, 1)
                    V.tensor_copy(col(dup, t, 2), psC[:, 0:2]).then_inc(dupc0, 1)
                dve.wait_ge(blk0, b + 1)
                dve.sem_inc(dve_step, 1)
                V.tensor_copy(agg[:, ds(b * D, D)], psF[:, 0:D]).then_inc(acc0, 1)
            dve.wait_ge(acc0, NB + 1)
            dve.wait_ge(dupc0, RING + 1)

            link(V.tensor_tensor(agg[:, :], agg[:, :], gs, ALU.add))
            link(V.tensor_tensor(blocks(agg[:, :]), blocks(agg[:, :]), spread(dinv[:, :]), ALU.mult))
            link(V.tensor_tensor(blocks(agg[:, :]), blocks(agg[:, :]),
                                 b12[:, 0:D].rearrange("p (a c) -> p a c", a=1).to_broadcast([P, NBP, D]), ALU.add))
            link(V.scalar_tensor_tensor(out=agg[:, :], in0=agg[:, :], scalar=0.0, in1=x_sb, op0=ALU.max, op1=ALU.add))
            link(V.tensor_scalar(dup, dup, 0.0, None, ALU.is_gt))
            link(V.tensor_scalar(tmaxb, srcf[:, :], -1.0, trash_f[:, 0:1], ALU.mult, ALU.add))
            link(V.tensor_tensor(tmaxb, tmaxb, dup, ALU.mult))
            link(V.tensor_tensor(tmaxb, tmaxb, srcf[:, :], ALU.add))
            link(V.tensor_copy(dsti[:, :], tmaxb))
            layernorm_relu(agg[:, :], hx, xc, 3)
            dve.wait_ge(zero_dma, 16 * 2 * GX)
            V.tensor_copy(blocks(acc[:, :], CX)[:, :, H:CX].rearrange("p b a -> p (b a)"), hist[:, :])
            with dve.Fori(0, NG) as q:
                dve.wait_ge(nM, q + 3 + NG)
                dve.wait_ge(tab_ready, q + 1)
                V.tensor_tensor(gat[:, ds((q % 2) * 512, 512)].rearrange("p (b c) -> p b c", c=C2),
                                psM[:, ds((q % 2) * 512, 512)].rearrange("p (b c) -> p b c", c=C2),
                                biasr[:, :].rearrange("p (a c) -> p a c", a=1).to_broadcast([P, GB, C2]),
                                ALU.add).then_inc(nE, 1)
            dve.wait_ge(tab_ready, 2 + NG)
            dve.sem_inc(sidx_ready, 1)

            for m in (valid1, oh1, ohb1, same1, sum1):
                dve.sem_inc(m, RING)
            with dve.Fori(0, NB) as b:
                s, e, f = pairs_of_block(dve, b)
                with dve.Fori(s, e) as j:
                    t = first_tile(dve, j, s, f)
                    V.tensor_scalar(valid[:, ds((j % RING) * 2, 2)], col(hif, t, 2), col(iota_f, b), None,
                                    ALU.is_equal).then_inc(valid1, 1)
                    dve.wait_ge(ohTp1, freed(j, RING))
                    for k in range(2):
                        ins = V.tensor_scalar(slot(ohb, j, k, P), iota_f[:, :], col(dstf, t + k),
                                              col(negblk, b), ALU.subtract, ALU.is_equal)
                    ins.then_inc(ohb1, 1)
                    dve.wait_ge(srcT1, done(j))
                    dve.wait_ge(comb1, freed(j, 1))
                    dve.wait_ge(valid1, done(j))
                    for k in range(2):
                        ins = V.tensor_scalar(same[:, k * P:(k + 1) * P], psS[:, k * P:(k + 1) * P],
                                              col(srcf, t + k), slot(valid, j, k, 1),
                                              ALU.is_equal, ALU.mult)
                    ins.then_inc(same1, 1)
                    dve.wait_ge(pre1, done(j))
                    dve.wait_ge(gath1, done(j))
                    dve.wait_ge(msg1, freed(j, NPS))
                    V.tensor_tensor(pre[:, ds((j % NPS) * 2 * C2, 2 * C2)], psP[:, 0:2 * C2],
                                    gat[:, ds((j % RING) * 2 * C2, 2 * C2)], ALU.add).then_inc(sum1, 1)
                    dve.wait_ge(fwd1, freed(j, 1))
                    for k in range(2):
                        ins = V.tensor_scalar(oh[:, k * P:(k + 1) * P], iota_f[:, :], col(dstf, t + k),
                                              col(negblk, b), ALU.subtract, ALU.is_equal)
                    ins.then_inc(oh1, 1)

            for q in range(NG):
                dve.wait_ge(fin_dma[q % 2], 16 * 2 * GX * (q // 2 + 1))
                a = acc[:, q * GB * CX:(q + 1) * GB * CX]
                for k in range(2 * GX):
                    at = ((q % 2) * 2 * GX + k) * GB * CX
                    ins = V.tensor_tensor(a, a, hx[:, at:at + GB * CX], ALU.add)
                    if k < 2 * GX - 1:
                        link(ins)
                ins.then_inc(fsum, 1)
                dve.wait_ge(fO, q + 1)
                o = xc[:, (q % 2) * GB * D:(q % 2 + 1) * GB * D]
                if q >= 2:
                    dve.wait_ge(out_dma, 16 * (q - 1))
                link(V.tensor_tensor(blocks(o), blocks(psC[:, 0:GB * D]),
                                     bn2r[:, :].rearrange("p (a c) -> p a c", a=1).to_broadcast([P, GB, D]), ALU.add))
                V.tensor_tensor(o, o, agg[:, q * GB * D:(q + 1) * GB * D], ALU.add).then_inc(fOut, 1)

        @block.tensor
        def _(pe):
            M = nc.tensor.matmul
            TR = nc.tensor.transpose
            pe.wait_ge(const, 15)
            pe.wait_ge(tabs_f, 1)
            pe.sem_inc(tile_c, 1)
            for c in range(TC):
                pe.wait_ge(tile_c, c + 1)
                TR(psS[:, 0:P], dstf[:, c * P:(c + 1) * P], ident[:, :]).then_inc(tile_t, 1)
                pe.wait_ge(tile_r, c + 1)
                TR(psS[:, P:2 * P], bounds[:, 0:1].to_broadcast([P, P]), ident[:, :]).then_inc(tile_t, 1)
                TR(psS[:, 2 * P:3 * P], bounds[:, 1:2].to_broadcast([P, P]), ident[:, :]).then_inc(tile_t, 1)
            pe.wait_ge(tile_r, TC + 1)
            M(psS[:, 0:P], bounds[:, 7:8].to_broadcast([P, P]), before[:, :], start=True, stop=True).then_inc(tile_t, 1)
            TR(psS[:, P:2 * P], bounds[:, 0:1].to_broadcast([P, P]), ident[:, :]).then_inc(tile_t, 1)

            pe.sem_inc(hmm, 2)
            M(psO[:, 0:NB], zb[:, :], zb[:, 0:NB], start=True, stop=False)
            with pe.Fori(0, (T + 3) // 4) as i:
                pe.wait_ge(hoh, i + 1)
                for u in range(4):
                    at = ((i % 2) * 4 + u) * 2 * P
                    ins = M(psO[:, 0:NB], ohb[:, ds(at, P)], ohb[:, ds(at + P, NB)], start=False, stop=False)
                ins.then_inc(hmm, 1)
            M(psO[:, 0:NB], zb[:, :], zb[:, 0:NB], start=False, stop=True).then_inc(hdone, 1)

            def node_groups(w, width, n0):
                for q in range(NG):
                    pe.wait_ge(nTs, q + (n0 + 1))
                    TR(psOT[:, (q % 2) * 512:(q % 2) * 512 + P], hx[:, q * P:(q + 1) * P], ident[:, :]).then_inc(nT, 1)
                    pe.wait_ge(nTs, q + (n0 + 3))
                    pe.wait_ge(nE, q + (n0 + 1))
                    M(psM[:, (q % 2) * 512:(q % 2) * 512 + width], ohT[:, (q % 2) * P:(q % 2 + 1) * P], w,
                      start=True, stop=True).then_inc(nM, 1)

            pe.sem_inc(nM, 2)
            pe.wait_ge(h_ready, 1)
            node_groups(W12[:, 0:P], P, 0)

            def source_rows(j, t):
                for k in range(2):
                    M(psS[:, k * P:(k + 1) * P], col(srcH, t + k).to_broadcast([P, P]), identb[:, :], start=True, stop=False)
                    ins = M(psS[:, k * P:(k + 1) * P], col(srcL, t + k).to_broadcast([P, P]), identb[:, :],
                            start=False, stop=True)
                return ins

            def open_sums(bank, width):
                M(bank[:, 0:width], zb[:, :], zb[:, 0:width], start=True, stop=False)

            def close_sums(bank, width):
                return M(bank[:, 0:width], zb[:, :], zb[:, 0:width], start=False, stop=True)

            for m in (srcT0, mm0, dup0):
                pe.sem_inc(m, RING)
            with pe.Fori(0, NB) as b:
                s, e, f = pairs_of_block(pe, b)
                pe.wait_ge(acc0, b + 1)
                pe.sem_inc(pe_step, 1)
                open_sums(psF, D)
                with pe.Fori(s, e) as j:
                    t = first_tile(pe, j, s, f)
                    pe.wait_ge(same0, freed(j, 1))
                    pe.sem_inc(pe_step, 1)
                    source_rows(j, t).then_inc(srcT0, 1)
                    pe.wait_ge(oh0, done(j))
                    pe.wait_ge(gath0, done(j))
                    pe.sem_inc(pe_step, 1)
                    for k in range(2):
                        ins = M(psF[:, 0:D], oh[:, k * P:(k + 1) * P],
                                gat[:, ds((j % RING) * 2 * C2 + k * C2, D)], start=False, stop=False)
                    ins.then_inc(mm0, 1)
                    pe.wait_ge(dupc0, freed(j, 1))
                    pe.wait_ge(same0, done(j))
                    pe.sem_inc(pe_step, 1)
                    for k in range(2):
                        ins = M(psC[:, k:k + 1], same[:, k * P:(k + 1) * P], ones[:, :],
                                start=True, stop=True)
                    ins.then_inc(dup0, 1)
                close_sums(psF, D).then_inc(blk0, 1)

            pe.wait_ge(h_ready, 2)
            node_groups(WBA[:, :], GB * C2, NG)

            for m in (srcT1, ohTp1, pre1, comb1, fwd1):
                pe.sem_inc(m, RING)
            with pe.Fori(0, NB) as b:
                s, e, f = pairs_of_block(pe, b)
                pe.wait_ge(tdst1, b + 1)
                pe.wait_ge(acc1, b + 1)
                pe.sem_inc(pe_step, 1)
                open_sums(psF, H)
                with pe.Fori(s, e) as j:
                    t = first_tile(pe, j, s, f)
                    pe.wait_ge(same1, freed(j, 1))
                    pe.sem_inc(pe_step, 1)
                    source_rows(j, t).then_inc(srcT1, 1)
                    pe.wait_ge(ohTs1, freed(j, 1))
                    pe.wait_ge(ohb1, done(j))
                    pe.sem_inc(pe_step, 1)
                    for k in range(2):
                        ins = M(psO[:, k * P:(k + 1) * P], slot(ohb, j, k, P), identb[:, :], start=True, stop=True)
                    ins.then_inc(ohTp1, 1)
                    pe.wait_ge(sum1, freed(j, 1))
                    pe.wait_ge(ohTs1, done(j))
                    pe.wait_ge(ea1, done(j))
                    pe.sem_inc(pe_step, 1)
                    for k in range(2):
                        M(psP[:, k * C2:(k + 1) * C2], ohT[:, k * P:(k + 1) * P], tdst[:, ds((b % 4) * C2, C2)],
                          start=True, stop=False)
                        ins = M(psP[:, k * C2:(k + 1) * C2], ea_at[:, :], WE[:, k * C2:(k + 1) * C2], start=False, stop=True)
                    ins.then_inc(pre1, 1)
                    pe.wait_ge(combs1, freed(j, 1))
                    pe.wait_ge(same1, done(j))
                    pe.wait_ge(msg1, done(j))
                    pe.sem_inc(pe_step, 1)
                    for k in range(2):
                        ins = M(psC[:, k * CX:(k + 1) * CX], same[:, k * P:(k + 1) * P],
                                msg[:, ds((j % NPS) * 2 * (C2 + 1) + k * (C2 + 1) + H, CX)], start=True, stop=True)
                    ins.then_inc(comb1, 1)
                    pe.wait_ge(oh1, done(j))
                    pe.sem_inc(pe_step, 1)
                    for k in range(2):
                        ins = M(psF[:, 0:H], oh[:, k * P:(k + 1) * P],
                                msg[:, ds((j % NPS) * 2 * (C2 + 1) + k * (C2 + 1), H)], start=False, stop=False)
                    ins.then_inc(fwd1, 1)
                close_sums(psF, H).then_inc(blk1, 1)

            for q in range(NG):
                pe.wait_ge(fsum, q + 1)
                if q:
                    pe.wait_ge(fS, q)
                for k in range(GB):
                    ins = TR(psT[0:CX, k * P:(k + 1) * P], acc[:, (q * GB + k) * CX:(q * GB + k + 1) * CX], ident[:, :])
                ins.then_inc(fT, 1)
                pe.wait_ge(fS, q + 1)
                if q:
                    pe.wait_ge(fFs, q)
                M(psM[0:H, 0:512], wf2x[:, :], pre[0:CX, :], start=True, stop=True).then_inc(fF, 1)
                pe.wait_ge(fFs, q + 1)
                if q:
                    pe.wait_ge(fHs, q)
                M(psP[0:H, :], wn1[:, :], gat[0:H, 0:512], start=True, stop=True).then_inc(fH, 1)
                pe.wait_ge(fHs, q + 1)
                if q:
                    pe.wait_ge(fOut, q)
                for k in range(GB):
                    ins = M(psC[:, k * D:(k + 1) * D], gat[0:H, 512 + k * P:512 + (k + 1) * P], wn2[:, :], start=True, stop=True)
                ins.then_inc(fO, 1)


def kernel(**inputs):
    import numpy as _np
    import concourse.bacc as _bacc
    from concourse import mybir as _mybir
    from concourse.bass_utils import run_bass_kernel_spmd as _run

    nc = _bacc.Bacc("TRN2", target_bir_lowering=False, num_devices=1)
    a = {k: _np.asarray(v) for k, v in inputs.items()}

    x = _np.zeros((NR, D), a["x"].dtype)
    x[:N] = a["x"]
    src = TRASH + _np.arange(TW * P, dtype=a["src"].dtype) % P
    src[:E] = a["src"]
    dst = _np.full(TW * P, -1, a["dst"].dtype)
    dst[:E] = a["dst"]
    ea = _np.zeros((TW * P, ED), a["edge_attr_16"].dtype)
    ea[:E] = a["edge_attr_16"]
    arrays = {
        "x": x.reshape(NBP, P, D).transpose(1, 0, 2).reshape(P, NBP * D),
        "src": src.reshape(TW, P).T,
        "dst": dst.reshape(TW, P).T,
        "ea": ea.reshape(TW, P, ED).transpose(0, 2, 1).reshape(TW * ED, P),
    }
    for k in ("W1", "b1", "W2", "b2"):
        arrays["l0_" + k] = a["L0_gnn_" + k]
    for k in ("Wf1", "bf1", "Wf2", "bf2", "Wn1", "bn1", "Wn2", "bn2"):
        arrays["l1_" + k] = a["L1_gnn_" + k]
    arrays = {f"in_{k}_dram": _np.ascontiguousarray(v) for k, v in arrays.items()}
    args = [nc.dram_tensor(k, v.shape, _mybir.dt.from_np(v.dtype), kind="ExternalInput").ap()
            for k, v in arrays.items()]
    out = nc.dram_tensor("out_0_dram", (P, NBP * D), _mybir.dt.float32, kind="ExternalOutput").ap()
    build(nc, *args, out)
    r = _run(nc, [arrays], core_ids=[0])
    y = r.results[0]["out_0_dram"]
    return _np.ascontiguousarray(y.reshape(P, NBP, D).transpose(1, 0, 2).reshape(NR, D)[:N])
```
